# Optimizing a Trainium2 kernel written in Bass

```python
import numpy as np
import jax
import jax.numpy as jnp

def _softmax(x, axis=-1):
    return jax.nn.softmax(x, axis=axis)

def _gelu(x):
    return jax.nn.gelu(x, approximate=True)

def _silu(x):
    return jax.nn.silu(x)

def _sigmoid(x):
    return jax.nn.sigmoid(x)

def _layernorm(x, axis=-1, eps=1e-05):
    m = jnp.mean(x, axis=axis, keepdims=True)
    v = jnp.var(x, axis=axis, keepdims=True)
    return (x - m) / jnp.sqrt(v + eps)

def _scatter_add(tgt, idx, src, axis=0):
    return tgt.at[idx].add(src)

def _segment_sum(src, seg, n):
    return jax.ops.segment_sum(src, seg, n)
kernel_name = 'mk_rec_standalone_d1_rec_r8_37c588'

def setup_inputs(seed: int=0):
    np.random.seed(seed)
    _w = jnp.asarray

    def _rec_inputs():
        import jax
        import jax.numpy as jnp
        _rk = jax.random.key(seed)
        r_behavior_embs = -0.000161372 + 0.999968 * jax.random.normal(jax.random.fold_in(_rk, 1), (2048, 200, 64), jnp.float32)
        r_pratical_seq_len = jax.random.randint(jax.random.fold_in(_rk, 2), (2048,), 1, 201, jnp.int32)
        return (r_behavior_embs, r_pratical_seq_len)
    r_behavior_embs, r_pratical_seq_len = _rec_inputs()

    def _L0_rec_setup():
        import jax, jax.numpy as jnp
        import numpy as np
        N, L, D, A, K = (1024, 200, 64, 5, 4)
        key = jax.random.key(seed)
        k1, k2, k3, k4, k5, k6 = jax.random.split(key, 6)
        return {'behavior_embs': jax.random.normal(k1, (N, L, D), dtype=jnp.float32), 'pratical_seq_len': jax.random.randint(k2, (N,), 1, L + 1), 'W1_w': jax.random.normal(k3, (A, D), dtype=jnp.float32) * (1.0 / np.sqrt(D)), 'W1_b': jax.random.normal(k4, (A,), dtype=jnp.float32) * 0.01, 'W2_w': jax.random.normal(k5, (K, A), dtype=jnp.float32) * (1.0 / np.sqrt(A)), 'W2_b': jax.random.normal(k6, (K,), dtype=jnp.float32) * 0.01}
    _L0_rec_all = _L0_rec_setup()
    _L0_rec_in = {k: v for k, v in _L0_rec_all.items() if k in ('W1_w', 'W1_b', 'W2_w', 'W2_b')}
    del _L0_rec_all
    return {'r_behavior_embs': r_behavior_embs, 'r_pratical_seq_len': r_pratical_seq_len, 'L0_rec_W1_w': _L0_rec_in['W1_w'], 'L0_rec_W1_b': _L0_rec_in['W1_b'], 'L0_rec_W2_w': _L0_rec_in['W2_w'], 'L0_rec_W2_b': _L0_rec_in['W2_b']}

def reference(r_behavior_embs, r_pratical_seq_len, L0_rec_W1_w, L0_rec_W1_b, L0_rec_W2_w, L0_rec_W2_b):
    import jax
    import jax.numpy as jnp

    def _L0_rec_ref(behavior_embs, pratical_seq_len, W1_w, W1_b, W2_w, W2_b):
        import jax, jax.numpy as jnp
        import numpy as np
        N, L, D, A, K = (1024, 200, 64, 5, 4)
        n, l, d = behavior_embs.shape
        valid = jnp.arange(l) < pratical_seq_len[:, None]
        h = behavior_embs
        s = jnp.tanh(jnp.einsum('nld,ad->nla', h, W1_w) + W1_b)
        s = jnp.einsum('nla,ka->nlk', s, W2_w) + W2_b
        s = jnp.where(valid[:, :, None], s, -jnp.inf)
        s = jnp.swapaxes(s, -1, -2)
        e = jnp.exp(s - jnp.max(s))
        denom = jnp.sum(e, axis=-1, keepdims=True)
        p = e / jnp.where(denom == 0, 1.0, denom)
        return jnp.einsum('nkl,nld->nkd', p, h)
    y = _L0_rec_ref(r_behavior_embs, r_pratical_seq_len, L0_rec_W1_w, L0_rec_W1_b, L0_rec_W2_w, L0_rec_W2_b)
    return y

_drawn_inputs = setup_inputs


def setup_inputs(seed=0):
    import zlib

    import numpy as np

    out = dict(_drawn_inputs(seed))
    spreads = {}
    factors = {'L0_rec_W1_b': 8.0, 'L0_rec_W2_b': 8.0}
    for name, (base, spread) in spreads.items():
        noise = np.random.default_rng([zlib.crc32(name.encode()), seed]).standard_normal(out[name].shape)
        drawn = base * np.exp(spread * noise) if base else spread * noise
        out[name] = jnp.asarray(drawn.astype(out[name].dtype))
    for name, factor in factors.items():
        out[name] = (out[name] * factor).astype(out[name].dtype)
    return out
```

```python
import concourse.bass as bass
from concourse import mybir
from contextlib import ExitStack

F32 = mybir.dt.float32
I32 = mybir.dt.int32
ALU = mybir.AluOpType
ACT = mybir.ActivationFunctionType
AX = mybir.AxisListType

N, L, D = 2048, 200, 64
A, K = 5, 4
P = 128
Q = 32
NQ = P // Q
SPAN = 40
T = L // SPAN
I = P // SPAN
PU = SPAN * I
G = 12
SLOTS = G * T
BS = G * I
NB = -(-N // BS)
LAST = N - BS
J = NQ
NJ = SLOTS // J
PAIRS = G // 2
ROWS = I * K
HB = D // Q
SH = 8
RING = 6
HALF = RING // 2
STORES = 16 * PAIRS * 2
LAG = 3
PEELED = LAG + RING
BIG = 1e30
MASK_PARTS = [6, 23, 40, NB]
assert SLOTS % J == 0 and (NB - PEELED) % RING == 0 and LAST >= 0 and D == 2 * Q

C_SAMPLE = 0
C_ONES = C_SAMPLE + I + 1
C_SEL = C_ONES + 2 * ROWS
C_W1 = C_SEL + 2 * T * K
C_W2 = C_W1 + NQ
C_TOKEN = C_W2 + 2 * NQ * J * 2
C_START = C_TOKEN + T
C_EYE = C_START + 1
C_HALVES = C_EYE + P
C_ROWS = C_HALVES + HB * P
C_HOLDS = C_ROWS + P
C_ALL = C_HOLDS + I * P


def shape_constants(np):
    c = np.zeros((P, C_ALL), np.float32)
    p = np.arange(P)
    used = p < PU
    for i in range(I):
        here = used & (p // SPAN == i)
        c[:, C_SAMPLE + i] = np.where(here, 0.0, -BIG)
        c[0, C_HOLDS + i * P:C_HOLDS + (i + 1) * P] = here
        for g in range(2):
            c[:, C_ONES + g * ROWS + i * K:C_ONES + g * ROWS + (i + 1) * K] = here[:, None]
    for q in range(NQ):
        c[Q * q:Q * q + Q, C_W1 + q] = 1
    row = p % Q
    for g in range(2):
        for k in range(K):
            mine = (row < 2 * ROWS) & (row // ROWS == g) & (row % K == k)
            for t in range(T):
                c[:, C_SEL + (t * 2 + g) * K + k] = mine
    for h in range(2):
        for q in range(NQ):
            for j in range(J):
                rows = slice(Q * j + A * q, Q * j + A * q + A)
                c[rows, C_W2 + (h * NQ + q) * 2 * J + (j // 2) * 4 + h * 2 + j % 2] = 1
    c[:, C_TOKEN:C_TOKEN + T] = np.arange(T) + 0.5
    c[:, C_START] = np.where(used, -T * (p % SPAN), 0)
    c[:, C_EYE:C_EYE + P] = np.eye(P)
    for b in range(HB):
        c[Q * b + p % Q, C_HALVES + b * P + p] = 1
    rows = p[row < NQ * A]
    c[rows % Q % A, C_ROWS + rows] = 1
    return c


def attention_pooling(nc, h, seq_len, w1, b1, w2, b2, consts, zeros, out):
    out_rows = out.rearrange("n k d -> (n k) d")

    def batch_of(first):
        return h[bass.ds(first, BS)].rearrange("(g i) (r t) d -> (i r) g (t d)", i=I, t=T)

    with ExitStack() as ctx:
        def sb(name, shape, dt=F32):
            return ctx.enter_context(nc.sbuf_tensor(name, shape, dt))

        def ps(name, width):
            return ctx.enter_context(nc.psum_tensor(name, [P, 512], F32))

        def sem(name):
            return ctx.enter_context(nc.semaphore(name))

        tokens = [sb(f"tokens{r}", [P, SLOTS * D]) for r in range(RING)]
        tokens_t = [sb(f"tokens_t{x}", [P, SLOTS * D]) for x in range(2)]
        hidden = [sb(f"hidden{x}", [P, NJ * Q]) for x in range(2)]
        scores = [sb(f"scores{x}", [P, J * 2 * SH * K]) for x in range(2)]
        token_mask = sb("token_mask", [P, NB * SLOTS])
        biased = sb("biased", [P, SLOTS * K])
        masked = [sb(f"masked{x}", [P, SLOTS * K + 1]) for x in range(2)]
        row_max = [sb(f"row_max{x}", [P, 1]) for x in range(2)]
        top = [sb(f"top{x}", [P, 1]) for x in range(2)]
        exp_bias = [sb(f"exp_bias{x}", [P, I + 1]) for x in range(2)]
        weights = [sb(f"weights{x}", [P, SLOTS * ROWS]) for x in range(2)]
        weights_plain = [sb(f"weights_plain{x}", [P, SLOTS * K]) for x in range(2)]
        own_sums = sb("own_sums", [P, 2 * 2 * T * K])
        denom = sb("denom", [P, 2])
        denom_safe = sb("denom_safe", [P, 2])
        inverse = [sb(f"inverse{x}", [P, 2]) for x in range(2)]
        pooled = [sb(f"pooled{x}", [P, HALF, 2 * 2 * D]) for x in range(2)]
        lengths = sb("lengths", [1, N], I32)
        lengths_f = sb("lengths_f", [1, N])
        left = sb("left", [P, NB * G])
        const = sb("const", [P, C_ALL])
        w1_turned = sb("w1_turned", [D, A])
        w2_b1_turned = sb("w2_b1_turned", [A, K + 1])
        w1_stat = sb("w1_stat", [P, HB * NQ * A])
        w2_stat = sb("w2_stat", [P, 2 * P])
        b1_rows = sb("b1_rows", [P, 1])
        b2_all = sb("b2_all", [P, K])

        layer1 = [ps(f"layer1_{x}", 512) for x in range(2)]
        layer2 = [ps(f"layer2_{x}", 512) for x in range(2)]
        sums = [ps(f"sums{x}", 512) for x in range(2)]
        denoms = [ps(f"denoms{x}", 512) for x in range(2)]

        loaded = [sem(f"loaded{r}") for r in range(RING)]
        loaded_first = [sem(f"loaded_first{j}") for j in range(J)]
        stored = [sem(f"stored{x}") for x in range(2)]
        small_loaded = sem("small_loaded")
        lengths_loaded = sem("lengths_loaded")
        b2_loaded = sem("b2_loaded")
        zeros_loaded = sem("zeros_loaded")
        cleared = sem("cleared")
        left_ready = sem("left_ready")
        lengths_ready = sem("lengths_ready")
        lengths_spread = sem("lengths_spread")
        weights_spread = sem("weights_spread")
        stationary_ready = sem("stationary_ready")
        transposed = sem("transposed")
        layer1_done = sem("layer1_done")
        hidden_ready = sem("hidden_ready")
        layer2_done = sem("layer2_done")
        scores_ready = sem("scores_ready")
        mask_step = sem("mask_step")
        biased_ready = sem("biased_ready")
        masked_ready = sem("masked_ready")
        row_max_ready = sem("row_max_ready")
        max_spread = sem("max_spread")
        top_ready = sem("top_ready")
        exp_bias_ready = sem("exp_bias_ready")
        weights_ready = sem("weights_ready")
        denoms_done = sem("denoms_done")
        sums_done = sem("sums_done")
        own_sums_ready = sem("own_sums_ready")
        denom_step = sem("denom_step")
        inverse_ready = sem("inverse_ready")
        pooled_ready = sem("pooled_ready")

        CLEARS = 2 * 3 + 2
        SMALL = 4 * 16
        LEFT_COLS = NB * G // 2
        ind_rows = const[:, C_ONES:C_ONES + 2 * ROWS]
        stationary1 = w1_stat[:, :].rearrange("p (b m) -> p b m", b=HB)
        stationary2 = w2_stat[:, :].rearrange("p (h m) -> p h m", h=2)

        def after(eng, s, count):
            if not isinstance(count, int) or count > 0:
                eng.wait_ge(s, count)

        def steps(eng, work, end):
            for n in range(PEELED):
                work(n, n % RING, n // RING)
            with eng.Fori(0, (NB - PEELED) // RING) as i:
                for u in range(PEELED, PEELED + RING):
                    work(i * RING + u, u % RING, i + u // RING)
            for n in range(NB, end):
                work(n, n % RING, n // RING)

        block = ctx.enter_context(nc.Block())

        @block.sync
        def _(sp):
            def load(r, first):
                sp.dma_start(tokens[r][0:PU, :].rearrange("p (g n) -> p g n", g=G),
                             batch_of(first)).then_inc(loaded[r], 16)

            def store(b, half, slot, n, first):
                sp.wait_ge(pooled_ready, b + 1)
                dst = out_rows[bass.ds(first * K, n * BS * K)].rearrange(
                    "(s c g r) d -> c g r s d", s=n, c=PAIRS, g=2)
                for pair in range(PAIRS):
                    c, region = pair % NQ, pair // NQ
                    for g in range(2):
                        src = pooled[half][Q * c + g * ROWS:Q * c + (g + 1) * ROWS, slot:slot + n,
                                           (2 * region + g) * D:(2 * region + g + 1) * D]
                        sp.dma_start(dst[pair, g], src).then_inc(stored[half], 16)

            sp.dma_start(const[:, :], consts).then_inc(small_loaded, 16)
            with nc.allow_non_contiguous_dma(reason="a few weights"):
                sp.dma_start(w1_turned[:, :], w1.rearrange("a d -> d a")).then_inc(small_loaded, 16)
                sp.dma_start(w2_b1_turned[:, 0:K], w2.rearrange("k a -> a k")).then_inc(small_loaded, 16)
                sp.dma_start(w2_b1_turned[:, K:], b1.unsqueeze(1)).then_inc(small_loaded, 16)
            for b in range(RING):
                if b:
                    load(b, b * BS)
                else:
                    for j in range(J):
                        g = G // J
                        sp.dma_start(tokens[0][0:PU, j * NJ * D:(j + 1) * NJ * D].rearrange("p (g n) -> p g n", g=g),
                                     batch_of(0)[:, j * g:(j + 1) * g, :]).then_inc(loaded_first[j], 16)
            with sp.Fori(0, NB // RING - 1) as i:
                for u in range(RING):
                    sp.wait_ge(sums_done, i * RING + (u + 1))
                    load(u, (i * RING + (RING + u)) * BS)
                    if u % HALF == HALF - 1:
                        store(i * RING + u, u // HALF, 0, HALF, (i * RING + (u - HALF + 1)) * BS)
            for b in range(NB // RING * RING, NB):
                sp.wait_ge(sums_done, b - RING + 1)
                load(b % RING, min(b * BS, LAST))
            store(NB - RING - 1, 0, 0, HALF, (NB - RING - HALF) * BS)
            store(NB - HALF - 1, 1, 0, HALF, (NB - 2 * HALF) * BS)
            store(NB - 2, 0, 0, HALF - 1, (NB - HALF) * BS)
            sp.wait_ge(stored[0], STORES * (NB // RING + 1))
            store(NB - 1, 0, HALF - 1, 1, LAST)
            sp.wait_ge(stored[0], STORES * (NB // RING + 2))
            sp.wait_ge(stored[1], STORES * (NB // RING))

        @block.gpsimd
        def _(pool):
            pool.wait_ge(left_ready, 2)
            pool.wait_ge(b2_loaded, 16)
            pool.wait_ge(small_loaded, SMALL)

            def make_mask(first, end):
                pairs = (end - first) * PAIRS
                cols = token_mask[:, first * SLOTS:end * SLOTS]
                nc.gpsimd.tensor_tensor(
                    cols.rearrange("p (c t g) -> p c t g", c=pairs, t=T),
                    left[:, first * G:end * G].rearrange("p (c g) -> p c g", g=2).unsqueeze(2).to_broadcast(
                        [P, pairs, T, 2]),
                    const[:, C_TOKEN:C_TOKEN + T].unsqueeze(1).unsqueeze(3).to_broadcast([P, pairs, T, 2]),
                    ALU.subtract).then_inc(mask_step, 1)
                made.append(end)
                pool.wait_ge(mask_step, 2 * len(made) - 1)
                nc.gpsimd.tensor_scalar(cols, cols, 0.0, 2 * BIG, ALU.min, ALU.mult).then_inc(mask_step, 1)

            made = []
            make_mask(0, MASK_PARTS[0])
            pool.wait_ge(mask_step, 2)

            def mask_scores(b, r, turn):
                x = r % 2
                pool.wait_ge(scores_ready, b + 1)
                nc.gpsimd.tensor_tensor(
                    biased[:, :].rearrange("p (h s k) -> p h s k", h=J // 2, k=K),
                    scores[x][:, :].rearrange("p (h s k) -> p h s k", h=J // 2, k=K)[:, :, 0:2 * NJ, :],
                    b2_all[:, :].unsqueeze(1).unsqueeze(1).to_broadcast([P, J // 2, 2 * NJ, K]), ALU.add
                ).then_inc(biased_ready, 1)
                pool.wait_ge(biased_ready, b + 1)
                after(pool, weights_ready, b - 1)
                nc.gpsimd.tensor_tensor(
                    masked[x][:, 0:SLOTS * K].rearrange("p (s k) -> p s k", k=K),
                    biased[:, :].rearrange("p (s k) -> p s k", k=K),
                    token_mask[:, bass.ds(b * SLOTS, SLOTS)].unsqueeze(2).to_broadcast([P, SLOTS, K]), ALU.add
                ).then_inc(masked_ready, 1)
                pool.wait_ge(top_ready, b + 1)
                nc.gpsimd.tensor_tensor(exp_bias[x][:, :], const[:, C_SAMPLE:C_SAMPLE + I + 1],
                                        top[x][:, 0:1].to_broadcast([P, I + 1]),
                                        ALU.subtract).then_inc(exp_bias_ready, 1)
                if isinstance(b, int) and b + 1 < len(MASK_PARTS):
                    make_mask(MASK_PARTS[b], MASK_PARTS[b + 1])
                    if b + 2 == len(MASK_PARTS):
                        pool.wait_ge(mask_step, 2 * len(MASK_PARTS))

            steps(pool, mask_scores, NB)

        @block.vector
        def _(dve):
            for banks, width in ((layer1, NJ * Q), (sums, 4 * D), (denoms, 4 * T * K)):
                for bank in banks:
                    nc.vector.memset(bank[:, 0:width], 0.0).then_inc(cleared, 1)
            for x in range(2):
                nc.vector.memset(masked[x][:, SLOTS * K:], -BIG / 10).then_inc(cleared, 1)

            dve.wait_ge(lengths_loaded, 16)
            nc.vector.tensor_copy(lengths_f[:, :], lengths[:, :]).then_inc(lengths_ready, 1)
            dve.wait_ge(small_loaded, SMALL)
            dve.wait_ge(weights_spread, 1)
            nc.vector.tensor_copy(b1_rows[:, :], layer1[1][:, HB * A + K:HB * A + K + 1]).then_inc(stationary_ready, 1)
            nc.vector.tensor_tensor(
                w1_stat[:, :].rearrange("p (b q a) -> p b q a", b=HB, q=NQ),
                layer1[1][:, 0:HB * A].rearrange("p (b a) -> p b a", b=HB).unsqueeze(2).to_broadcast([P, HB, NQ, A]),
                const[:, C_W1:C_W1 + NQ].unsqueeze(1).unsqueeze(3).to_broadcast([P, HB, NQ, A]),
                ALU.mult).then_inc(stationary_ready, 1)
            places = 2 * NQ * J * 2
            nc.vector.tensor_tensor(
                w2_stat[:, :].rearrange("p (m k) -> p m k", k=K),
                layer1[1][:, HB * A:HB * A + K].unsqueeze(1).to_broadcast([P, places, K]),
                const[:, C_W2:C_W2 + places].unsqueeze(2).to_broadcast([P, places, K]),
                ALU.mult).then_inc(stationary_ready, 1)
            dve.wait_ge(zeros_loaded, RING * 16)

            dve.wait_ge(cleared, CLEARS)

            def transpose_tokens(b, r, j):
                cols = slice(j * NJ * D, (j + 1) * NJ * D)
                nc.vector.transpose(tokens_t[r % 2][:, cols], tokens[r][:, cols]).then_inc(transposed, 1)

            def step(n, r, turn):
                x = r % 2
                tr = not isinstance(n, int) or n < NB
                sc = not isinstance(n, int) or 2 <= n < NB + 2
                dn = not isinstance(n, int) or 3 <= n
                y = (r + 1) % 2
                if sc:
                    dve.wait_ge(layer2_done, n - 1)
                    after(dve, masked_ready, n - 3)
                    nc.vector.transpose(
                        scores[x][:, :].rearrange("p (m s k) -> p s m k", m=J, s=SH),
                        layer2[x][:, 0:SH * Q].rearrange("p (s m k) -> p s m k", s=SH, m=J)).then_inc(scores_ready, 1)
                if tr:
                    if isinstance(n, int) and n == 0:
                        dve.wait_ge(loaded_first[0], 16)
                    else:
                        dve.wait_ge(loaded[r], turn * 16 if r == 0 else turn * 16 + 16)
                    after(dve, layer1_done, n - 1)
                    transpose_tokens(n, r, 0)
                    if isinstance(n, int) and n == 0:
                        dve.wait_ge(loaded_first[1], 16)
                    transpose_tokens(n, r, 1)
                if sc:
                    dve.wait_ge(masked_ready, n - 1)
                    nc.vector.reduce_max(row_max[x][:, :], masked[x][:, :], AX.X).then_inc(row_max_ready, 1)
                if dn:
                    dve.wait_ge(denoms_done, n - 2)
                    nc.vector.tensor_tensor(
                        own_sums[:, :].rearrange("p (r s) -> p r s", r=2),
                        denoms[y][:, 0:4 * T * K].rearrange("p (r s) -> p r s", r=2),
                        const[:, C_SEL:C_SEL + 2 * T * K].unsqueeze(1).to_broadcast([P, 2, 2 * T * K]),
                        ALU.mult).then_inc(own_sums_ready, 1)
                if tr:
                    if isinstance(n, int) and n == 0:
                        dve.wait_ge(loaded_first[2], 16)
                    transpose_tokens(n, r, 2)
                if dn:
                    dve.wait_ge(own_sums_ready, n - 2)
                    nc.vector.reduce_sum(denom[:, :], own_sums[:, :].rearrange("p (r s) -> p r s", r=2),
                                         AX.X).then_inc(denom_step, 1)
                if tr:
                    if isinstance(n, int) and n == 0:
                        dve.wait_ge(loaded_first[3], 16)
                    transpose_tokens(n, r, 3)
                if sc:
                    dve.wait_ge(max_spread, n - 1)
                    nc.vector.reduce_max(top[x][:, :], layer2[x][:, SH * Q:SH * Q + P], AX.X).then_inc(top_ready, 1)
                if dn:
                    dve.wait_ge(denom_step, 2 * n - 5)
                    nc.vector.scalar_tensor_tensor(denom_safe[:, :], denom[:, :], 0.0, denom[:, :],
                                                   ALU.is_equal, ALU.add).then_inc(denom_step, 1)
                    dve.wait_ge(denom_step, 2 * n - 4)
                    after(dve, pooled_ready, n - 3)
                    nc.vector.reciprocal(inverse[y][:, :], denom_safe[:, :]).then_inc(inverse_ready, 1)

            steps(dve, step, NB + LAG)

        @block.tensor
        def _(pe):
            def step(n, r, turn):
                x = r % 2
                layers = not isinstance(n, int) or n < NB
                summed = not isinstance(n, int) or n >= 2
                if layers:
                    after(pe, hidden_ready, n - 1)
                    for j in range(J):
                        half = tokens_t[x][:, j // 2 * 2 * NJ * D:(j // 2 + 1) * 2 * NJ * D].rearrange(
                            "p (c g t b r) -> p g b c t r", g=2, t=T, b=HB, r=Q)
                        if j % 2 == 0:
                            pe.wait_ge(transposed, n * J + (j + 2))
                        for b in range(HB):
                            rhs = half[:, j % 2, b]
                            last = nc.tensor.matmul(layer1[x][Q * j:Q * j + NQ * A, 0:NJ * Q], stationary1[:, b, :], rhs,
                                                    start=(b == 0), stop=(b == HB - 1), tile_position=(0, Q * j))
                    last.then_inc(layer1_done, 1)
                if summed:
                    buf = tokens[(r - 2) % RING][:, :].rearrange("p (c g t d) -> p c g t d", c=PAIRS, g=2, t=T)
                    w = weights[x][:, :].rearrange("p (c t m) -> p c t m", c=PAIRS, t=T)
                    plain = weights_plain[x][:, :].rearrange("p (c s) -> p c s", c=PAIRS)
                    pe.wait_ge(weights_ready, n - 1)
                    after(pe, own_sums_ready, n - 3)
                    for c in range(NQ):
                        regions = 2 if c + NQ < PAIRS else 1
                        last = nc.tensor.matmul(denoms[x][Q * c:Q * c + 2 * ROWS, 0:regions * 2 * T * K], ind_rows,
                                                plain[:, c:c + NQ * (regions - 1) + 1:NQ, :],
                                                start=True, stop=True, tile_position=(0, Q * c))
                    last.then_inc(denoms_done, 1)
                    after(pe, pooled_ready, n - 3)
                    for region, pairs in ((0, NQ), (1, PAIRS - NQ)):
                        for t in range(T):
                            for c in range(pairs):
                                pair = region * NQ + c
                                last = nc.tensor.matmul(
                                    sums[x][Q * c:Q * c + 2 * ROWS, region * 2 * D:(region + 1) * 2 * D],
                                    w[:, pair, t, :], buf[:, pair, :, t, :],
                                    start=(t == 0), stop=(t == T - 1), tile_position=(0, Q * c))
                    last.then_inc(sums_done, 1)
                if not isinstance(n, int) or 1 <= n < NB + 1:
                    pe.wait_ge(row_max_ready, n)
                    nc.tensor.transpose(layer2[1 - x][:, SH * Q:SH * Q + P], row_max[1 - x][:, 0:1].to_broadcast([P, P]),
                                        const[:, C_EYE:C_EYE + P]).then_inc(max_spread, 1)
                if layers:
                    pe.wait_ge(hidden_ready, n + 1)
                    after(pe, top_ready, n - 1)
                    for half, n_slots in ((0, SH), (1, NJ - SH)):
                        last = nc.tensor.matmul(layer2[x][:, 0:n_slots * Q], stationary2[:, half, :],
                                                hidden[x][:, half * SH * Q:(half * SH + n_slots) * Q],
                                                start=(half == 0), stop=(half == 1))
                    last.then_inc(layer2_done, 1)

            pe.wait_ge(cleared, CLEARS)
            pe.wait_ge(small_loaded, SMALL)
            for b in range(HB):
                nc.tensor.matmul(layer1[1][:, b * A:(b + 1) * A], const[0:D, C_HALVES + b * P:C_HALVES + (b + 1) * P],
                                 w1_turned[:, :], start=True, stop=True)
            nc.tensor.matmul(layer1[1][:, HB * A:HB * A + K + 1], const[0:A, C_ROWS:C_ROWS + P],
                             w2_b1_turned[:, :], start=True, stop=True).then_inc(weights_spread, 1)
            pe.wait_ge(lengths_ready, 1)
            whole = (NB - 1) * G
            for bank, parts in enumerate((((0, LEFT_COLS, 0),), ((0, whole - LEFT_COLS, LEFT_COLS * I),
                                                                 (whole - LEFT_COLS, G, LAST)))):
                for at, n, first in parts:
                    for i in range(I):
                        last = nc.tensor.matmul(layer2[bank][:, at:at + n], const[0:1, C_HOLDS + i * P:C_HOLDS + (i + 1) * P],
                                                lengths_f[0:1, first + i:first + i + I * (n - 1) + 1:I],
                                                start=(i == 0), stop=(i == I - 1))
                last.then_inc(lengths_spread, 1)
            pe.wait_ge(stationary_ready, 3)
            pe.wait_ge(left_ready, 2)
            steps(pe, step, NB + 2)

        @block.scalar
        def _(act):
            act.dma_start(lengths[:, :], seq_len.unsqueeze(0)).then_inc(lengths_loaded, 16)
            act.dma_start(b2_all[:, :], b2.unsqueeze(0).to_broadcast([P, K])).then_inc(b2_loaded, 16)
            for r in range(RING):
                act.dma_start(tokens[r][PU:P, :], zeros).then_inc(zeros_loaded, 16)
            act.wait_ge(small_loaded, SMALL)
            for part in range(2):
                act.wait_ge(lengths_spread, part + 1)
                nc.scalar.activation(left[:, part * LEFT_COLS:(part + 1) * LEFT_COLS], layer2[part][:, 0:LEFT_COLS],
                                     ACT.Identity, bias=const[:, C_START:C_START + 1]).then_inc(left_ready, 1)
            act.wait_ge(stationary_ready, 3)

            def step(n, r, turn):
                x, y = r % 2, (r + 1) % 2
                if not isinstance(n, int) or 1 <= n < NB + 1:
                    act.wait_ge(layer1_done, n)
                    after(act, layer2_done, n - 2)
                    nc.scalar.activation(hidden[y][:, :], layer1[y][:, 0:NJ * Q], ACT.Tanh,
                                         bias=b1_rows[:, 0:1]).then_inc(hidden_ready, 1)
                if not isinstance(n, int) or 2 <= n < NB + 2:
                    act.wait_ge(exp_bias_ready, n - 1)
                    after(act, sums_done, n - 3)
                    source = masked[x][:, 0:SLOTS * K].rearrange("p (s k) -> p s k", k=K)
                    for i in range(I):
                        nc.scalar.activation(
                            weights[x][:, :].rearrange("p (s i k) -> p s i k", i=I, k=K)[:, :, i, :],
                            source, ACT.Exp, bias=exp_bias[x][:, i:i + 1])
                    nc.scalar.activation(weights_plain[x][:, :], masked[x][:, 0:SLOTS * K], ACT.Exp,
                                         bias=exp_bias[x][:, I:I + 1]).then_inc(weights_ready, 1)
                if not isinstance(n, int) or 3 <= n:
                    act.wait_ge(sums_done, n - 2)
                    act.wait_ge(inverse_ready, n - 2)
                    half, slot = (r - LAG) % RING // HALF, (r - LAG) % HALF
                    after(act, stored[half], (turn - (1 if r < LAG else 0)) * STORES)
                    for region in range(2):
                        ins = nc.scalar.activation(pooled[half][:, slot, region * 2 * D:(region + 1) * 2 * D],
                                                   sums[y][:, region * 2 * D:(region + 1) * 2 * D], ACT.Copy,
                                                   scale=inverse[y][:, region:region + 1])
                    ins.then_inc(pooled_ready, 1)

            steps(act, step, NB + LAG)


_INS = ["r_behavior_embs", "r_pratical_seq_len", "L0_rec_W1_w", "L0_rec_W1_b", "L0_rec_W2_w", "L0_rec_W2_b"]


def kernel(**inputs):
    import numpy as _np
    import concourse.bacc as _bacc
    from concourse import mybir as _mybir
    from concourse.bass_utils import run_bass_kernel_spmd as _run

    nc = _bacc.Bacc("TRN2", target_bir_lowering=False, num_devices=1)
    arrays = {f"in_{name}_dram": _np.ascontiguousarray(inputs[name]) for name in _INS}
    arrays["in_consts_dram"] = shape_constants(_np)
    arrays["in_zeros_dram"] = _np.zeros((P - PU, SLOTS * D), _np.float32)
    args = [nc.dram_tensor(name, a.shape, _mybir.dt.from_np(a.dtype), kind="ExternalInput").ap()
            for name, a in arrays.items()]
    args.append(nc.dram_tensor("out_0_dram", (N, K, D), F32, kind="ExternalOutput").ap())
    attention_pooling(nc, *args)
    r = _run(nc, [arrays], core_ids=[0])
    return r.results[0]["out_0_dram"]
```

```python
import concourse.bass as bass
from concourse import mybir
from contextlib import ExitStack

F32 = mybir.dt.float32
I32 = mybir.dt.int32
ALU = mybir.AluOpType
ACT = mybir.ActivationFunctionType
AX = mybir.AxisListType

N, L, D = 2048, 200, 64
A, K = 5, 4
P = 128
Q = 32
NQ = P // Q
SPAN = 40
T = L // SPAN
I = P // SPAN
PU = SPAN * I
G = 12
SLOTS = G * T
BS = G * I
NB = -(-N // BS)
LAST = N - BS
J = NQ
NJ = SLOTS // J
PAIRS = G // 2
SINGLES = G - 2 * NQ
ROWS = I * K
HB = D // Q
SH = 8
RING = 6
HALF = RING // 2
STORES = 16 * G
LAG = 3
PEELED = LAG + RING
BIG = 1e30
MASK_PARTS = [6, 13, 20, 27, 34, 41, 48, NB]
assert SINGLES == NQ and SLOTS % J == 0 and (NB - PEELED) % RING == 0 and LAST >= 0 and D == 2 * Q

C_SAMPLE = 0
C_ONES = C_SAMPLE + I + 1
C_SEL = C_ONES + 2 * ROWS
C_W1 = C_SEL + 2 * 2 * T * K
C_W2 = C_W1 + NQ
C_TOKEN = C_W2 + 2 * NQ * J * 2
C_START = C_TOKEN + T
C_EYE = C_START + 1
C_HALVES = C_EYE + P
C_ROWS = C_HALVES + HB * P
C_HOLDS = C_ROWS + P
C_ALL = C_HOLDS + I * P


def shape_constants(np):
    c = np.zeros((P, C_ALL), np.float32)
    p = np.arange(P)
    used = p < PU
    for i in range(I):
        here = used & (p // SPAN == i)
        c[:, C_SAMPLE + i] = np.where(here, 0.0, -BIG)
        c[0, C_HOLDS + i * P:C_HOLDS + (i + 1) * P] = here
        for g in range(2):
            c[:, C_ONES + g * ROWS + i * K:C_ONES + g * ROWS + (i + 1) * K] = here[:, None]
    for q in range(NQ):
        c[Q * q:Q * q + Q, C_W1 + q] = 1
    row, tile = p % Q, p // Q
    for g in range(2):
        for k in range(K):
            paired = (row < 2 * ROWS) & (row // ROWS == g) & (row % K == k)
            single = (row < ROWS) & (tile % 2 == g) & (row % K == k)
            for t in range(T):
                c[:, C_SEL + (t * 2 + g) * K + k] = paired
                c[:, C_SEL + ((T + t) * 2 + g) * K + k] = single
    for h in range(2):
        for q in range(NQ):
            for j in range(J):
                rows = slice(Q * j + A * q, Q * j + A * q + A)
                c[rows, C_W2 + (h * NQ + q) * 2 * J + (j // 2) * 4 + h * 2 + j % 2] = 1
    c[:, C_TOKEN:C_TOKEN + T] = np.arange(T) + 0.5
    c[:, C_START] = np.where(used, -T * (p % SPAN), 0)
    c[:, C_EYE:C_EYE + P] = np.eye(P)
    for b in range(HB):
        c[Q * b + p % Q, C_HALVES + b * P + p] = 1
    rows = p[row < NQ * A]
    c[rows % Q % A, C_ROWS + rows] = 1
    return c


def attention_pooling(nc, h, seq_len, w1, b1, w2, b2, consts, zeros, out):
    out_rows = out.rearrange("n k d -> (n k) d")

    def batch_of(first):
        return h[bass.ds(first, BS)].rearrange("(g i) (r t) d -> (i r) g (t d)", i=I, t=T)

    with ExitStack() as ctx:
        def sb(name, shape, dt=F32):
            return ctx.enter_context(nc.sbuf_tensor(name, shape, dt))

        def ps(name, width):
            return ctx.enter_context(nc.psum_tensor(name, [P, 512], F32))

        def sem(name):
            return ctx.enter_context(nc.semaphore(name))

        tokens = [sb(f"tokens{r}", [P, SLOTS * D]) for r in range(RING)]
        tokens_t = [sb(f"tokens_t{x}", [P, SLOTS * D]) for x in range(2)]
        hidden = [sb(f"hidden{x}", [P, NJ * Q]) for x in range(2)]
        scores = [sb(f"scores{x}", [P, J * 2 * SH * K]) for x in range(2)]
        token_mask = sb("token_mask", [P, NB * SLOTS])
        biased = sb("biased", [P, SLOTS * K])
        masked = [sb(f"masked{x}", [P, SLOTS * K + 1]) for x in range(2)]
        row_max = [sb(f"row_max{x}", [P, 1]) for x in range(2)]
        top = [sb(f"top{x}", [P, 1]) for x in range(2)]
        exp_bias = [sb(f"exp_bias{x}", [P, I + 1]) for x in range(2)]
        weights = [sb(f"weights{x}", [P, SLOTS * ROWS]) for x in range(2)]
        weights_plain = [sb(f"weights_plain{x}", [P, SLOTS * K]) for x in range(2)]
        all_sums = sb("all_sums", [P, 2 * 2 * T * K])
        own_sums = sb("own_sums", [P, 2 * 2 * T * K])
        denom = sb("denom", [P, 2])
        denom_safe = sb("denom_safe", [P, 2])
        inverse = [sb(f"inverse{x}", [P, 2]) for x in range(2)]
        pooled = [sb(f"pooled{x}", [P, HALF, 3 * D]) for x in range(2)]
        lengths = sb("lengths", [1, N], I32)
        lengths_f = sb("lengths_f", [1, N])
        left = sb("left", [P, NB * G])
        const = sb("const", [P, C_ALL])
        w1_turned = sb("w1_turned", [D, A])
        w2_b1_turned = sb("w2_b1_turned", [A, K + 1])
        w1_stat = sb("w1_stat", [P, HB * NQ * A])
        w2_stat = sb("w2_stat", [P, 2 * P])
        b1_rows = sb("b1_rows", [P, 1])
        b2_all = sb("b2_all", [P, K])

        layer1 = [ps(f"layer1_{x}", 512) for x in range(2)]
        layer2 = [ps(f"layer2_{x}", 512) for x in range(2)]
        sums = [ps(f"sums{x}", 512) for x in range(2)]
        denoms = [ps(f"denoms{x}", 512) for x in range(2)]

        loaded = [sem(f"loaded{r}") for r in range(RING)]
        loaded_first = [sem(f"loaded_first{j}") for j in range(J)]
        stored = [sem(f"stored{x}") for x in range(2)]
        small_loaded = sem("small_loaded")
        lengths_loaded = sem("lengths_loaded")
        b2_loaded = sem("b2_loaded")
        zeros_loaded = sem("zeros_loaded")
        cleared = sem("cleared")
        left_ready = sem("left_ready")
        lengths_ready = sem("lengths_ready")
        lengths_spread = sem("lengths_spread")
        weights_spread = sem("weights_spread")
        stationary_ready = sem("stationary_ready")
        transposed = sem("transposed")
        layer1_done = sem("layer1_done")
        hidden_ready = sem("hidden_ready")
        layer2_done = sem("layer2_done")
        scores_ready = sem("scores_ready")
        mask_step = sem("mask_step")
        biased_ready = sem("biased_ready")
        masked_ready = sem("masked_ready")
        row_max_ready = sem("row_max_ready")
        max_spread = sem("max_spread")
        top_ready = sem("top_ready")
        exp_bias_ready = sem("exp_bias_ready")
        weights_ready = sem("weights_ready")
        denoms_done = sem("denoms_done")
        sums_done = sem("sums_done")
        all_sums_ready = sem("all_sums_ready")
        own_sums_ready = sem("own_sums_ready")
        denom_ready = sem("denom_ready")
        denom_safe_ready = sem("denom_safe_ready")
        inverse_ready = sem("inverse_ready")
        pooled_ready = sem("pooled_ready")

        CLEARS = 2 * 3 + 2
        SMALL = 4 * 16
        LEFT_COLS = NB * G // 2
        ind_rows = const[:, C_ONES:C_ONES + 2 * ROWS]
        stationary1 = w1_stat[:, :].rearrange("p (b m) -> p b m", b=HB)
        stationary2 = w2_stat[:, :].rearrange("p (h m) -> p h m", h=2)

        def after(eng, s, count):
            if not isinstance(count, int) or count > 0:
                eng.wait_ge(s, count)

        def steps(eng, work, end):
            for n in range(PEELED):
                work(n, n % RING, n // RING)
            with eng.Fori(0, (NB - PEELED) // RING) as i:
                for u in range(PEELED, PEELED + RING):
                    work(i * RING + u, u % RING, i + u // RING)
            for n in range(NB, end):
                work(n, n % RING, n // RING)

        block = ctx.enter_context(nc.Block())

        @block.sync
        def _(sp):
            def load(r, first):
                sp.dma_start(tokens[r][0:PU, :].rearrange("p (g n) -> p g n", g=G),
                             batch_of(first)).then_inc(loaded[r], 16)

            def store(b, half, slot, n, first):
                sp.wait_ge(pooled_ready, b + 1)
                dst = out_rows[bass.ds(first * K, n * BS * K)].rearrange(
                    "(s g r) d -> g r s d", s=n, g=G)
                for g in range(G):
                    c, row, col = (g // 2, g % 2 * ROWS, g % 2 * D) if g < 2 * NQ else (g - 2 * NQ, 0, 2 * D)
                    src = pooled[half][Q * c + row:Q * c + row + ROWS, slot:slot + n, col:col + D]
                    sp.dma_start(dst[g], src).then_inc(stored[half], 16)

            sp.dma_start(const[:, :], consts).then_inc(small_loaded, 16)
            with nc.allow_non_contiguous_dma(reason="a few weights"):
                sp.dma_start(w1_turned[:, :], w1.rearrange("a d -> d a")).then_inc(small_loaded, 16)
                sp.dma_start(w2_b1_turned[:, 0:K], w2.rearrange("k a -> a k")).then_inc(small_loaded, 16)
                sp.dma_start(w2_b1_turned[:, K:], b1.unsqueeze(1)).then_inc(small_loaded, 16)
            for b in range(RING):
                if b:
                    load(b, b * BS)
                else:
                    for j in range(J):
                        g = G // J
                        sp.dma_start(tokens[0][0:PU, j * NJ * D:(j + 1) * NJ * D].rearrange("p (g n) -> p g n", g=g),
                                     batch_of(0)[:, j * g:(j + 1) * g, :]).then_inc(loaded_first[j], 16)
            with sp.Fori(0, NB // RING - 1) as i:
                for u in range(RING):
                    sp.wait_ge(sums_done, i * RING + (u + 1))
                    load(u, (i * RING + (RING + u)) * BS)
                    if u % HALF == HALF - 1:
                        store(i * RING + u, u // HALF, 0, HALF, (i * RING + (u - HALF + 1)) * BS)
            for b in range(NB // RING * RING, NB):
                sp.wait_ge(sums_done, b - RING + 1)
                load(b % RING, min(b * BS, LAST))
            store(NB - RING - 1, 0, 0, HALF, (NB - RING - HALF) * BS)
            store(NB - HALF - 1, 1, 0, HALF, (NB - 2 * HALF) * BS)
            store(NB - 2, 0, 0, HALF - 1, (NB - HALF) * BS)
            sp.wait_ge(stored[0], STORES * (NB // RING + 1))
            store(NB - 1, 0, HALF - 1, 1, LAST)
            sp.wait_ge(stored[0], STORES * (NB // RING + 2))
            sp.wait_ge(stored[1], STORES * (NB // RING))

        @block.gpsimd
        def _(pool):
            pool.wait_ge(left_ready, 2)
            pool.wait_ge(b2_loaded, 16)
            pool.wait_ge(small_loaded, SMALL)

            def make_mask(first, end):
                pairs = (end - first) * PAIRS
                cols = token_mask[:, first * SLOTS:end * SLOTS]
                nc.gpsimd.tensor_tensor(
                    cols.rearrange("p (c t g) -> p c t g", c=pairs, t=T),
                    left[:, first * G:end * G].rearrange("p (c g) -> p c g", g=2).unsqueeze(2).to_broadcast(
                        [P, pairs, T, 2]),
                    const[:, C_TOKEN:C_TOKEN + T].unsqueeze(1).unsqueeze(3).to_broadcast([P, pairs, T, 2]),
                    ALU.subtract).then_inc(mask_step, 1)
                made.append(end)
                pool.wait_ge(mask_step, 2 * len(made) - 1)
                nc.gpsimd.tensor_scalar(cols, cols, 0.0, 2 * BIG, ALU.min, ALU.mult).then_inc(mask_step, 1)

            made = []
            make_mask(0, MASK_PARTS[0])
            pool.wait_ge(mask_step, 2)

            def select_sums(b):
                pool.wait_ge(all_sums_ready, b + 1)
                after(pool, denom_ready, b)
                nc.gpsimd.tensor_tensor(own_sums[:, :], all_sums[:, :], const[:, C_SEL:C_SEL + 4 * T * K],
                                        ALU.mult).then_inc(own_sums_ready, 1)

            def mask_scores(b, r, turn):
                x = r % 2
                pool.wait_ge(scores_ready, b + 1)
                nc.gpsimd.tensor_tensor(
                    biased[:, :].rearrange("p (h s k) -> p h s k", h=J // 2, k=K),
                    scores[x][:, :].rearrange("p (h s k) -> p h s k", h=J // 2, k=K)[:, :, 0:2 * NJ, :],
                    b2_all[:, :].unsqueeze(1).unsqueeze(1).to_broadcast([P, J // 2, 2 * NJ, K]), ALU.add
                ).then_inc(biased_ready, 1)
                pool.wait_ge(biased_ready, b + 1)
                after(pool, weights_ready, b - 1)
                nc.gpsimd.tensor_tensor(
                    masked[x][:, 0:SLOTS * K].rearrange("p (s k) -> p s k", k=K),
                    biased[:, :].rearrange("p (s k) -> p s k", k=K),
                    token_mask[:, bass.ds(b * SLOTS, SLOTS)].unsqueeze(2).to_broadcast([P, SLOTS, K]), ALU.add
                ).then_inc(masked_ready, 1)
                if not isinstance(b, int) or b >= 1:
                    select_sums(b - 1)
                pool.wait_ge(top_ready, b + 1)
                nc.gpsimd.tensor_tensor(exp_bias[x][:, :], const[:, C_SAMPLE:C_SAMPLE + I + 1],
                                        top[x][:, 0:1].to_broadcast([P, I + 1]),
                                        ALU.subtract).then_inc(exp_bias_ready, 1)
                if isinstance(b, int) and b + 1 < len(MASK_PARTS):
                    make_mask(MASK_PARTS[b], MASK_PARTS[b + 1])
                    if b + 2 == len(MASK_PARTS):
                        pool.wait_ge(mask_step, 2 * len(MASK_PARTS))

            steps(pool, mask_scores, NB)
            select_sums(NB - 1)

        @block.vector
        def _(dve):
            for banks, width in ((layer1, NJ * Q), (sums, 3 * D), (denoms, 4 * T * K)):
                for bank in banks:
                    nc.vector.memset(bank[:, 0:width], 0.0).then_inc(cleared, 1)
            for x in range(2):
                nc.vector.memset(masked[x][:, SLOTS * K:], -BIG / 10).then_inc(cleared, 1)

            dve.wait_ge(lengths_loaded, 16)
            nc.vector.tensor_copy(lengths_f[:, :], lengths[:, :]).then_inc(lengths_ready, 1)
            dve.wait_ge(small_loaded, SMALL)
            dve.wait_ge(weights_spread, 1)
            nc.vector.tensor_copy(b1_rows[:, :], layer1[1][:, HB * A + K:HB * A + K + 1]).then_inc(stationary_ready, 1)
            nc.vector.tensor_tensor(
                w1_stat[:, :].rearrange("p (b q a) -> p b q a", b=HB, q=NQ),
                layer1[1][:, 0:HB * A].rearrange("p (b a) -> p b a", b=HB).unsqueeze(2).to_broadcast([P, HB, NQ, A]),
                const[:, C_W1:C_W1 + NQ].unsqueeze(1).unsqueeze(3).to_broadcast([P, HB, NQ, A]),
                ALU.mult).then_inc(stationary_ready, 1)
            places = 2 * NQ * J * 2
            nc.vector.tensor_tensor(
                w2_stat[:, :].rearrange("p (m k) -> p m k", k=K),
                layer1[1][:, HB * A:HB * A + K].unsqueeze(1).to_broadcast([P, places, K]),
                const[:, C_W2:C_W2 + places].unsqueeze(2).to_broadcast([P, places, K]),
                ALU.mult).then_inc(stationary_ready, 1)
            dve.wait_ge(zeros_loaded, RING * 16)

            dve.wait_ge(cleared, CLEARS)

            def transpose_tokens(r, first, end):
                cols = slice(first * NJ * D, end * NJ * D)
                nc.vector.transpose(tokens_t[r % 2][:, cols], tokens[r][:, cols]).then_inc(transposed, 1)

            def invert(m, y):
                dve.wait_ge(denom_safe_ready, m + 1)
                after(dve, pooled_ready, m - 1)
                nc.vector.reciprocal(inverse[y][:, :], denom_safe[:, :]).then_inc(inverse_ready, 1)

            def step(n, r, turn):
                x, y = r % 2, (r + 1) % 2
                steady = not isinstance(n, int)
                tokens_here = steady or n < NB
                scores_here = steady or 2 <= n < NB + 2
                denoms_here = steady or 3 <= n
                if scores_here:
                    dve.wait_ge(layer2_done, n - 1)
                    after(dve, masked_ready, n - 3)
                    nc.vector.transpose(
                        scores[x][:, :].rearrange("p (m s k) -> p s m k", m=J, s=SH),
                        layer2[x][:, 0:SH * Q].rearrange("p (s m k) -> p s m k", s=SH, m=J)).then_inc(scores_ready, 1)
                if steady or 4 <= n <= NB:
                    invert(n - 4, x)
                if tokens_here:
                    if steady or n:
                        dve.wait_ge(loaded[r], turn * 16 if r == 0 else turn * 16 + 16)
                    else:
                        dve.wait_ge(loaded_first[0], 16)
                        dve.wait_ge(loaded_first[1], 16)
                    after(dve, layer1_done, n - 1)
                    transpose_tokens(r, 0, 2)
                if scores_here:
                    dve.wait_ge(masked_ready, n - 1)
                    nc.vector.reduce_max(row_max[x][:, :], masked[x][:, :], AX.X).then_inc(row_max_ready, 1)
                if tokens_here:
                    if not steady and n == 0:
                        dve.wait_ge(loaded_first[2], 16)
                    transpose_tokens(r, 2, 3)
                if scores_here:
                    dve.wait_ge(max_spread, n - 1)
                    nc.vector.reduce_max(top[x][:, :], layer2[x][:, SH * Q:SH * Q + P], AX.X).then_inc(top_ready, 1)
                if denoms_here:
                    dve.wait_ge(own_sums_ready, n - 2)
                    nc.vector.reduce_sum(denom[:, :], own_sums[:, :].rearrange("p (r s) -> p r s", r=2),
                                         AX.X).then_inc(denom_ready, 1)
                if tokens_here:
                    if not steady and n == 0:
                        dve.wait_ge(loaded_first[3], 16)
                    transpose_tokens(r, 3, 4)
                if denoms_here:
                    dve.wait_ge(denom_ready, n - 2)
                    after(dve, inverse_ready, n - 3)
                    nc.vector.scalar_tensor_tensor(denom_safe[:, :], denom[:, :], 0.0, denom[:, :],
                                                   ALU.is_equal, ALU.add).then_inc(denom_safe_ready, 1)
                if not steady and n >= NB:
                    invert(n - 3, y)

            steps(dve, step, NB + LAG)

        @block.tensor
        def _(pe):
            def step(n, r, turn):
                x = r % 2
                steady = not isinstance(n, int)
                layers = steady or n < NB
                summed = steady or n >= 2
                if layers:
                    after(pe, hidden_ready, n - 1)
                    for j in range(J):
                        half = tokens_t[x][:, j // 2 * 2 * NJ * D:(j // 2 + 1) * 2 * NJ * D].rearrange(
                            "p (c g t b r) -> p g b c t r", g=2, t=T, b=HB, r=Q)
                        if j % 2 == 0:
                            pe.wait_ge(transposed, n * 3 + (1 if j == 0 else 3))
                        for b in range(HB):
                            rhs = half[:, j % 2, b]
                            last = nc.tensor.matmul(layer1[x][Q * j:Q * j + NQ * A, 0:NJ * Q], stationary1[:, b, :], rhs,
                                                    start=(b == 0), stop=(b == HB - 1), tile_position=(0, Q * j))
                    last.then_inc(layer1_done, 1)
                if summed:
                    buf = tokens[(r - 2) % RING][:, :].rearrange("p (c g t d) -> p c g t d", c=PAIRS, g=2, t=T)
                    w = weights[x][:, :].rearrange("p (c t m) -> p c t m", c=PAIRS, t=T)
                    plain = weights_plain[x][:, :].rearrange("p (c s) -> p c s", c=PAIRS)
                    pe.wait_ge(weights_ready, n - 1)
                    after(pe, all_sums_ready, n - 3)
                    for c in range(NQ):
                        single = NQ + c // 2
                        last = nc.tensor.matmul(denoms[x][Q * c:Q * c + 2 * ROWS, 0:4 * T * K], ind_rows,
                                                plain[:, c:single + 1:single - c, :],
                                                start=True, stop=True, tile_position=(0, Q * c))
                    last.then_inc(denoms_done, 1)
                    after(pe, pooled_ready, n - 3)
                    for t in range(T):
                        for c in range(NQ):
                            nc.tensor.matmul(sums[x][Q * c:Q * c + 2 * ROWS, 0:2 * D], w[:, c, t, :], buf[:, c, :, t, :],
                                             start=(t == 0), stop=(t == T - 1), tile_position=(0, Q * c))
                if steady or 1 <= n < NB + 1:
                    pe.wait_ge(row_max_ready, n)
                    nc.tensor.transpose(layer2[1 - x][:, SH * Q:SH * Q + P], row_max[1 - x][:, 0:1].to_broadcast([P, P]),
                                        const[:, C_EYE:C_EYE + P]).then_inc(max_spread, 1)
                if summed:
                    for t in range(T):
                        for c in range(NQ):
                            pair, g = NQ + c // 2, c % 2
                            last = nc.tensor.matmul(sums[x][Q * c:Q * c + ROWS, 2 * D:3 * D],
                                                    w[:, pair, t, g * ROWS:(g + 1) * ROWS], buf[:, pair, g, t, :],
                                                    start=(t == 0), stop=(t == T - 1), tile_position=(0, Q * c))
                    last.then_inc(sums_done, 1)
                if layers:
                    pe.wait_ge(hidden_ready, n + 1)
                    after(pe, top_ready, n - 1)
                    for half, n_slots in ((0, SH), (1, NJ - SH)):
                        last = nc.tensor.matmul(layer2[x][:, 0:n_slots * Q], stationary2[:, half, :],
                                                hidden[x][:, half * SH * Q:(half * SH + n_slots) * Q],
                                                start=(half == 0), stop=(half == 1))
                    last.then_inc(layer2_done, 1)

            pe.wait_ge(cleared, CLEARS)
            pe.wait_ge(small_loaded, SMALL)
            for b in range(HB):
                nc.tensor.matmul(layer1[1][:, b * A:(b + 1) * A], const[0:D, C_HALVES + b * P:C_HALVES + (b + 1) * P],
                                 w1_turned[:, :], start=True, stop=True)
            nc.tensor.matmul(layer1[1][:, HB * A:HB * A + K + 1], const[0:A, C_ROWS:C_ROWS + P],
                             w2_b1_turned[:, :], start=True, stop=True).then_inc(weights_spread, 1)
            pe.wait_ge(lengths_ready, 1)
            whole = (NB - 1) * G
            for bank, parts in enumerate((((0, LEFT_COLS, 0),), ((0, whole - LEFT_COLS, LEFT_COLS * I),
                                                                 (whole - LEFT_COLS, G, LAST)))):
                for at, n, first in parts:
                    for i in range(I):
                        last = nc.tensor.matmul(layer2[bank][:, at:at + n], const[0:1, C_HOLDS + i * P:C_HOLDS + (i + 1) * P],
                                                lengths_f[0:1, first + i:first + i + I * (n - 1) + 1:I],
                                                start=(i == 0), stop=(i == I - 1))
                last.then_inc(lengths_spread, 1)
            pe.wait_ge(stationary_ready, 3)
            pe.wait_ge(left_ready, 2)
            steps(pe, step, NB + 2)

        @block.scalar
        def _(act):
            act.dma_start(lengths[:, :], seq_len.unsqueeze(0)).then_inc(lengths_loaded, 16)
            act.dma_start(b2_all[:, :], b2.unsqueeze(0).to_broadcast([P, K])).then_inc(b2_loaded, 16)
            for r in range(RING):
                act.dma_start(tokens[r][PU:P, :], zeros).then_inc(zeros_loaded, 16)
            act.wait_ge(small_loaded, SMALL)
            for part in range(2):
                act.wait_ge(lengths_spread, part + 1)
                nc.scalar.activation(left[:, part * LEFT_COLS:(part + 1) * LEFT_COLS], layer2[part][:, 0:LEFT_COLS],
                                     ACT.Identity, bias=const[:, C_START:C_START + 1]).then_inc(left_ready, 1)
            act.wait_ge(stationary_ready, 3)

            def step(n, r, turn):
                x, y = r % 2, (r + 1) % 2
                if not isinstance(n, int) or 1 <= n < NB + 1:
                    act.wait_ge(layer1_done, n)
                    after(act, layer2_done, n - 2)
                    nc.scalar.activation(hidden[y][:, :], layer1[y][:, 0:NJ * Q], ACT.Tanh,
                                         bias=b1_rows[:, 0:1]).then_inc(hidden_ready, 1)
                if not isinstance(n, int) or 3 <= n:
                    act.wait_ge(denoms_done, n - 2)
                    after(act, own_sums_ready, n - 3)
                    nc.scalar.copy(all_sums[:, :], denoms[y][:, 0:4 * T * K]).then_inc(all_sums_ready, 1)
                if not isinstance(n, int) or 2 <= n < NB + 2:
                    act.wait_ge(exp_bias_ready, n - 1)
                    after(act, sums_done, n - 3)
                    source = masked[x][:, 0:SLOTS * K].rearrange("p (s k) -> p s k", k=K)
                    for i in range(I):
                        nc.scalar.activation(
                            weights[x][:, :].rearrange("p (s i k) -> p s i k", i=I, k=K)[:, :, i, :],
                            source, ACT.Exp, bias=exp_bias[x][:, i:i + 1])
                    nc.scalar.activation(weights_plain[x][:, :], masked[x][:, 0:SLOTS * K], ACT.Exp,
                                         bias=exp_bias[x][:, I:I + 1]).then_inc(weights_ready, 1)
                if not isinstance(n, int) or 3 <= n:
                    act.wait_ge(sums_done, n - 2)
                    act.wait_ge(inverse_ready, n - 2)
                    half, slot = (r - LAG) % RING // HALF, (r - LAG) % HALF
                    after(act, stored[half], (turn - (1 if r < LAG else 0)) * STORES)
                    for part, cols in enumerate((slice(0, 2 * D), slice(2 * D, 3 * D))):
                        ins = nc.scalar.activation(pooled[half][:, slot, cols], sums[y][:, cols], ACT.Copy,
                                                   scale=inverse[y][:, part:part + 1])
                    ins.then_inc(pooled_ready, 1)

            steps(act, step, NB + LAG)


_INS = ["r_behavior_embs", "r_pratical_seq_len", "L0_rec_W1_w", "L0_rec_W1_b", "L0_rec_W2_w", "L0_rec_W2_b"]


def kernel(**inputs):
    import numpy as _np
    import concourse.bacc as _bacc
    from concourse import mybir as _mybir
    from concourse.bass_utils import run_bass_kernel_spmd as _run

    nc = _bacc.Bacc("TRN2", target_bir_lowering=False, num_devices=1)
    arrays = {f"in_{name}_dram": _np.ascontiguousarray(inputs[name]) for name in _INS}
    arrays["in_consts_dram"] = shape_constants(_np)
    arrays["in_zeros_dram"] = _np.zeros((P - PU, SLOTS * D), _np.float32)
    args = [nc.dram_tensor(name, a.shape, _mybir.dt.from_np(a.dtype), kind="ExternalInput").ap()
            for name, a in arrays.items()]
    args.append(nc.dram_tensor("out_0_dram", (N, K, D), F32, kind="ExternalOutput").ap())
    attention_pooling(nc, *args)
    r = _run(nc, [arrays], core_ids=[0])
    return r.results[0]["out_0_dram"]
```

```python
import concourse.bass as bass
from concourse import mybir
from contextlib import ExitStack

F32 = mybir.dt.float32
I32 = mybir.dt.int32
ALU = mybir.AluOpType
ACT = mybir.ActivationFunctionType
AX = mybir.AxisListType

N, L, D = 2048, 200, 64
A, K = 5, 4
P = 128
Q = 32
NQ = P // Q
SPAN = 40
T = L // SPAN
I = P // SPAN
PU = SPAN * I
G = 12
SLOTS = G * T
BS = G * I
NB = -(-N // BS)
LAST = N - BS
AGAIN = NB * BS - N
J = NQ
NJ = SLOTS // J
PAIRS = G // 2
SINGLES = G - 2 * NQ
ROWS = I * K
HB = D // Q
SH = 8
RING = 6
HALF = RING // 2
STORES = 16 * G
POOL_STORES = (3, 4)
LAG = 3
PEELED = LAG + RING
BIG = 1e30
EARLY = 6
assert SINGLES == NQ and SLOTS % J == 0 and (NB - PEELED) % RING == 0 and LAST >= 0 and D == 2 * Q

C_SAMPLE = 0
C_ONES = C_SAMPLE + I + 1
C_SEL = C_ONES + 2 * ROWS
C_W1 = C_SEL + 2 * 2 * T * K
C_W2 = C_W1 + NQ
C_TOKEN = C_W2 + 2 * NQ * J * 2
C_START = C_TOKEN + T
C_EYE = C_START + 1
C_ALL = C_EYE + P
R_HIDDEN = 0
R_HOLDS = R_HIDDEN + P
R_ALL = R_HOLDS + I * P


def shape_constants(np):
    c = np.zeros((P, C_ALL), np.float32)
    few = np.zeros((A, R_ALL), np.float32)
    p = np.arange(P)
    used = p < PU
    for i in range(I):
        here = used & (p // SPAN == i)
        c[:, C_SAMPLE + i] = np.where(here, 0.0, -BIG)
        few[0, R_HOLDS + i * P:R_HOLDS + (i + 1) * P] = here
        for g in range(2):
            c[:, C_ONES + g * ROWS + i * K:C_ONES + g * ROWS + (i + 1) * K] = here[:, None]
    for q in range(NQ):
        c[Q * q:Q * q + Q, C_W1 + q] = 1
    row, tile = p % Q, p // Q
    for g in range(2):
        for k in range(K):
            paired = (row < 2 * ROWS) & (row // ROWS == g) & (row % K == k)
            single = (row < ROWS) & (tile % 2 == g) & (row % K == k)
            for t in range(T):
                c[:, C_SEL + (t * 2 + g) * K + k] = paired
                c[:, C_SEL + ((T + t) * 2 + g) * K + k] = single
    for h in range(2):
        for q in range(NQ):
            for j in range(J):
                rows = slice(Q * j + A * q, Q * j + A * q + A)
                c[rows, C_W2 + (h * NQ + q) * 2 * J + (j // 2) * 4 + h * 2 + j % 2] = 1
    c[:, C_TOKEN:C_TOKEN + T] = np.arange(T) + 0.5
    c[:, C_START] = np.where(used, -T * (p % SPAN), 0)
    c[:, C_EYE:C_EYE + P] = np.eye(P)
    rows = p[row < NQ * A]
    few[rows % Q % A, R_HIDDEN + rows] = 1
    return c, few


def attention_pooling(nc, h, seq_len, w1, b1, w2, b2, consts, few_consts, zeros, out):
    out_rows = out.rearrange("n k d -> (n k) d")

    def batch_of(first):
        return h[bass.ds(first, BS)].rearrange("(g i) (r t) d -> (i r) g (t d)", i=I, t=T)

    with ExitStack() as ctx:
        def sb(name, shape, dt=F32):
            return ctx.enter_context(nc.sbuf_tensor(name, shape, dt))

        def ps(name):
            return ctx.enter_context(nc.psum_tensor(name, [P, 512], F32))

        def sem(name):
            return ctx.enter_context(nc.semaphore(name))

        tokens = [sb(f"tokens{r}", [P, SLOTS * D]) for r in range(RING)]
        tokens_t = [sb(f"tokens_t{x}", [P, SLOTS * D]) for x in range(2)]
        hidden = [sb(f"hidden{x}", [P, NJ * Q]) for x in range(2)]
        scores = [sb(f"scores{x}", [P, J * 2 * SH * K]) for x in range(2)]
        missing = sb("missing", [P, SLOTS])
        token_mask = sb("token_mask", [P, SLOTS])
        bias_and_mask = sb("bias_and_mask", [P, SLOTS * K])
        masked = [sb(f"masked{x}", [P, SLOTS * K + 1]) for x in range(2)]
        row_max = [sb(f"row_max{x}", [P, 1]) for x in range(2)]
        top = [sb(f"top{x}", [P, 1]) for x in range(2)]
        exp_bias = [sb(f"exp_bias{x}", [P, I + 1]) for x in range(2)]
        weights = [sb(f"weights{x}", [P, SLOTS * ROWS]) for x in range(2)]
        weights_plain = [sb(f"weights_plain{x}", [P, SLOTS * K]) for x in range(2)]
        all_sums = sb("all_sums", [P, 2 * 2 * T * K])
        own_sums = sb("own_sums", [P, 2 * 2 * T * K])
        added = sb("added", [P, 2 * 2 * T * K])
        denom = sb("denom", [P, 2])
        denom_safe = sb("denom_safe", [P, 2])
        inverse = [sb(f"inverse{x}", [P, 2]) for x in range(2)]
        pooled = [sb(f"pooled{x}", [P, HALF, 3 * D]) for x in range(2)]
        lengths = sb("lengths", [1, N], I32)
        lengths_f = sb("lengths_f", [1, N])
        left = sb("left", [P, NB * G])
        const = sb("const", [P, C_ALL])
        few_const = sb("few_const", [A, R_ALL])
        w1_rows = sb("w1_rows", [A, D])
        w2_b1_turned = sb("w2_b1_turned", [A, K + 1])
        w1_stat = sb("w1_stat", [P, HB * NQ * A])
        w2_stat = sb("w2_stat", [P, 2 * P])
        b1_rows = sb("b1_rows", [P, 1])
        b2_all = sb("b2_all", [P, K])

        layer1 = [ps(f"layer1_{x}") for x in range(2)]
        layer2 = [ps(f"layer2_{x}") for x in range(2)]
        sums = [ps(f"sums{x}") for x in range(2)]
        denoms = [ps(f"denoms{x}") for x in range(2)]

        loaded = [[sem(f"loaded{r}_half{half}") for half in range(2)] for r in range(RING)]
        stored = [sem(f"stored{x}") for x in range(2)]
        last_stored = sem("last_stored")
        last_stored_pool = sem("last_stored_pool")
        small_loaded = sem("small_loaded")
        lengths_loaded = sem("lengths_loaded")
        b2_loaded = sem("b2_loaded")
        cleared = sem("cleared")
        zeros_loaded = sem("zeros_loaded")
        sides_cleared = sem("sides_cleared")
        left_ready = sem("left_ready")
        lengths_ready = sem("lengths_ready")
        lengths_spread = sem("lengths_spread")
        weights_spread = sem("weights_spread")
        stationary_ready = sem("stationary_ready")
        transposed = sem("transposed")
        layer1_done = sem("layer1_done")
        hidden_ready = sem("hidden_ready")
        layer2_done = sem("layer2_done")
        scores_ready = sem("scores_ready")
        missing_ready = sem("missing_ready")
        mask_ready = sem("mask_ready")
        bias_and_mask_ready = sem("bias_and_mask_ready")
        masked_ready = sem("masked_ready")
        row_max_ready = sem("row_max_ready")
        max_spread = sem("max_spread")
        top_ready = sem("top_ready")
        exp_bias_ready = sem("exp_bias_ready")
        weights_ready = sem("weights_ready")
        denoms_done = sem("denoms_done")
        sums_done = sem("sums_done")
        all_sums_ready = sem("all_sums_ready")
        own_sums_ready = sem("own_sums_ready")
        denom_ready = sem("denom_ready")
        denom_safe_ready = sem("denom_safe_ready")
        inverse_ready = sem("inverse_ready")
        pooled_ready = sem("pooled_ready")

        CLEARS = 2 * 2 + 2
        SMALL = 5 * 16
        whole = (NB - 1) * G
        rest = (whole - EARLY * G) // 2
        left_parts = [[(0, EARLY * G, 0)],
                      [(EARLY * G, rest, EARLY * BS)],
                      [(EARLY * G + rest, rest, EARLY * BS + rest * I), (whole, G, LAST)]]
        ind_rows = const[:, C_ONES:C_ONES + 2 * ROWS]
        stationary1 = w1_stat[:, :].rearrange("p (b m) -> p b m", b=HB)
        stationary2 = w2_stat[:, :].rearrange("p (h m) -> p h m", h=2)

        def after(eng, s, count):
            if not isinstance(count, int) or count > 0:
                eng.wait_ge(s, count)

        def steps(eng, work, end, peeled_end=0):
            loop_end = NB - peeled_end
            for n in range(PEELED):
                work(n, n % RING, n // RING)
            with eng.Fori(0, (loop_end - PEELED) // RING) as i:
                for u in range(PEELED, PEELED + RING):
                    work(i * RING + u, u % RING, i + u // RING)
            for n in range(loop_end, end):
                work(n, n % RING, n // RING)

        def store(eng, half, slot, n, first, signal, groups=range(G), skipped=0):
            dst = out_rows[bass.ds(first * K, n * BS * K)].rearrange("(s g r) d -> g r s d", s=n, g=G)
            for g in groups:
                c, row, col = (g // 2, g % 2 * ROWS, g % 2 * D) if g < 2 * NQ else (g - 2 * NQ, 0, 2 * D)
                skip = max(skipped - g * I, 0) * K
                if skip < ROWS:
                    src = pooled[half][Q * c + row + skip:Q * c + row + ROWS, slot:slot + n, col:col + D]
                    eng.dma_start(dst[g, skip:ROWS], src).then_inc(signal, 16)

        block = ctx.enter_context(nc.Block())

        @block.sync
        def _(sp):
            def load_groups(r, first, half, start, end):
                sp.dma_start(tokens[r][0:PU, start * T * D:end * T * D].rearrange("p (g n) -> p g n", g=end - start),
                             batch_of(first)[:, start:end, :]).then_inc(loaded[r][half], 16)

            def load(r, first, skipped=0):
                load_groups(r, first, 0, skipped, G // 2)
                load_groups(r, first, 1, G // 2, G)

            load_groups(0, 0, 0, 0, G // 4)
            load_groups(0, 0, 0, G // 4, G // 2)
            sp.dma_start(const[:, :], consts).then_inc(small_loaded, 16)
            load_groups(0, 0, 1, G // 2, G)
            sp.dma_start(few_const[:, :], few_consts).then_inc(small_loaded, 16)
            for b in range(1, RING):
                sp.wait_ge(sides_cleared, b)
                load(b, b * BS)

            def step(m, u):
                sp.wait_ge(sums_done, m + 1)
                if isinstance(m, int) and m + RING == NB - 1:
                    load(u, LAST, skipped=AGAIN // I)
                else:
                    load(u, (m + RING) * BS)
                part = u % HALF
                if part < 2 and (not isinstance(m, int) or m >= HALF):
                    sp.wait_ge(pooled_ready, m - part)
                    half = (u // HALF + 1) % 2
                    store(sp, half, 0, HALF, (m - part - HALF) * BS, stored[half],
                          groups=range(part * G // 2, (part + 1) * G // 2))

            for m in range(RING):
                step(m, m)
            with sp.Fori(1, NB // RING - 1) as i:
                for u in range(RING):
                    step(i * RING + u, u)
            for m in range(NB // RING * RING - RING, NB - RING):
                step(m, m % RING)
            for b in range(NB - RING - 1, NB - 1, HALF):
                sp.wait_ge(pooled_ready, b + 1)
                store(sp, b % RING // HALF, 0, HALF, (b - HALF + 1) * BS, stored[b % RING // HALF])
            sp.wait_ge(pooled_ready, NB - 1)
            store(sp, 0, 0, HALF - 1, (NB - HALF) * BS, last_stored, groups=range(G - POOL_STORES[0]))
            sp.wait_ge(pooled_ready, NB)
            store(sp, 0, HALF - 1, 1, LAST, last_stored, groups=range(G - POOL_STORES[1]), skipped=AGAIN)
            sp.wait_ge(stored[0], STORES * (NB // RING))
            sp.wait_ge(stored[1], STORES * (NB // RING))
            sp.wait_ge(last_stored, 16 * (2 * G - sum(POOL_STORES) - AGAIN // I))

        @block.gpsimd
        def _(pool):
            edge = P - Q
            for r in range(1, RING):
                nc.gpsimd.memset(tokens[r][edge:P, :], 0.0).then_inc(sides_cleared, 1)
            pool.wait_ge(sides_cleared, RING - 1)
            pool.wait_ge(cleared, CLEARS)
            pool.wait_ge(b2_loaded, 16)
            pool.wait_ge(small_loaded, SMALL)

            def count_missing(b):
                nc.gpsimd.tensor_tensor(
                    missing[:, :].rearrange("p (c t g) -> p c t g", c=PAIRS, t=T),
                    left[:, bass.ds(b * G, G)].rearrange("p (c g) -> p c g", g=2).unsqueeze(2).to_broadcast(
                        [P, PAIRS, T, 2]),
                    const[:, C_TOKEN:C_TOKEN + T].unsqueeze(1).unsqueeze(3).to_broadcast([P, PAIRS, T, 2]),
                    ALU.subtract).then_inc(missing_ready, 1)

            def make_mask():
                nc.gpsimd.tensor_scalar(token_mask[:, :], missing[:, :], 0.0, 2 * BIG,
                                        ALU.min, ALU.mult).then_inc(mask_ready, 1)

            def add_bias_to_mask(b):
                pool.wait_ge(mask_ready, b + 1)
                after(pool, masked_ready, b)
                nc.gpsimd.tensor_tensor(
                    bias_and_mask[:, :].rearrange("p (s k) -> p s k", k=K),
                    token_mask[:, :].unsqueeze(2).to_broadcast([P, SLOTS, K]),
                    b2_all[:, :].unsqueeze(1).to_broadcast([P, SLOTS, K]), ALU.add).then_inc(bias_and_mask_ready, 1)

            def select_sums(b):
                pool.wait_ge(all_sums_ready, b + 1)
                after(pool, denom_ready, b * 2)
                nc.gpsimd.tensor_tensor(own_sums[:, :], all_sums[:, :], const[:, C_SEL:C_SEL + 4 * T * K],
                                        ALU.mult).then_inc(own_sums_ready, 1)

            def bias_exponentials(b, x):
                pool.wait_ge(top_ready, b + 1)
                nc.gpsimd.tensor_tensor(exp_bias[x][:, :], const[:, C_SAMPLE:C_SAMPLE + I + 1],
                                        top[x][:, 0:1].to_broadcast([P, I + 1]),
                                        ALU.subtract).then_inc(exp_bias_ready, 1)

            def mask_scores(b, r, turn):
                x = r % 2
                steady = not isinstance(b, int)
                pool.wait_ge(scores_ready, b + 1)
                pool.wait_ge(bias_and_mask_ready, b + 1)
                after(pool, weights_ready, b - 1)
                nc.gpsimd.tensor_tensor(
                    masked[x][:, 0:SLOTS * K].rearrange("p (h s k) -> p h s k", h=J // 2, k=K),
                    scores[x][:, :].rearrange("p (h s k) -> p h s k", h=J // 2, k=K)[:, :, 0:2 * NJ, :],
                    bias_and_mask[:, :].rearrange("p (h s k) -> p h s k", h=J // 2, k=K), ALU.add
                ).then_inc(masked_ready, 1)
                if not steady and b + 1 == EARLY:
                    pool.wait_ge(left_ready, 3)
                if steady or b < NB - 1:
                    count_missing(b + 1)
                    pool.wait_ge(missing_ready, b + 2)
                if not steady and b >= NB - 2:
                    bias_exponentials(b, x)
                if steady or b >= 1:
                    select_sums(b - 1)
                if steady or b < NB - 1:
                    make_mask()
                if steady or b < NB - 2:
                    bias_exponentials(b, x)
                if steady or b < NB - 1:
                    add_bias_to_mask(b + 1)

            pool.wait_ge(left_ready, 1)
            count_missing(0)
            pool.wait_ge(missing_ready, 1)
            make_mask()
            add_bias_to_mask(0)
            steps(pool, mask_scores, NB, peeled_end=RING)
            select_sums(NB - 1)
            pool.wait_ge(pooled_ready, NB - 1)
            store(pool, 0, 0, HALF - 1, (NB - HALF) * BS, last_stored_pool, groups=range(G - POOL_STORES[0], G))
            pool.wait_ge(pooled_ready, NB)
            store(pool, 0, HALF - 1, 1, LAST, last_stored_pool, groups=range(G - POOL_STORES[1], G))
            pool.wait_ge(last_stored_pool, 16 * sum(POOL_STORES))

        @block.vector
        def _(dve):
            for banks, width in ((layer1, NJ * Q), (denoms, 4 * T * K)):
                for bank in banks:
                    nc.vector.memset(bank[:, 0:width], 0.0).then_inc(cleared, 1)
            for x in range(2):
                nc.vector.memset(masked[x][:, SLOTS * K:], -BIG / 10).then_inc(cleared, 1)
            dve.wait_ge(cleared, CLEARS)
            dve.wait_ge(lengths_loaded, 16)
            nc.vector.tensor_copy(lengths_f[:, :], lengths[:, :]).then_inc(lengths_ready, 1)

            def place_weights():
                dve.wait_ge(small_loaded, SMALL)
                dve.wait_ge(weights_spread, 1)
                nc.vector.tensor_copy(b1_rows[:, :], layer1[1][:, HB * A + K:HB * A + K + 1]).then_inc(stationary_ready, 1)
                nc.vector.tensor_tensor(
                    w1_stat[:, :].rearrange("p (b q a) -> p b q a", b=HB, q=NQ),
                    layer1[1][:, 0:HB * A].rearrange("p (b a) -> p b a", b=HB).unsqueeze(2).to_broadcast([P, HB, NQ, A]),
                    const[:, C_W1:C_W1 + NQ].unsqueeze(1).unsqueeze(3).to_broadcast([P, HB, NQ, A]),
                    ALU.mult).then_inc(stationary_ready, 1)
                places = 2 * NQ * J * 2
                nc.vector.tensor_tensor(
                    w2_stat[:, :].rearrange("p (m k) -> p m k", k=K),
                    layer1[1][:, HB * A:HB * A + K].unsqueeze(1).to_broadcast([P, places, K]),
                    const[:, C_W2:C_W2 + places].unsqueeze(2).to_broadcast([P, places, K]),
                    ALU.mult).then_inc(stationary_ready, 1)

            def transpose_tokens(r, first, end):
                cols = slice(first * NJ * D, end * NJ * D)
                nc.vector.transpose(tokens_t[r % 2][:, cols], tokens[r][:, cols]).then_inc(transposed, 1)

            def scores_from_layer(b, x):
                dve.wait_ge(layer2_done, b + 1)
                after(dve, masked_ready, b - 1)
                nc.vector.transpose(
                    scores[x][:, :].rearrange("p (m s k) -> p s m k", m=J, s=SH),
                    layer2[x][:, 0:SH * Q].rearrange("p (s m k) -> p s m k", s=SH, m=J)).then_inc(scores_ready, 1)

            def max_of_partition(b, x):
                dve.wait_ge(masked_ready, b + 1)
                nc.vector.reduce_max(row_max[x][:, :], masked[x][:, :], AX.X).then_inc(row_max_ready, 1)

            def max_of_batch(b, x):
                dve.wait_ge(max_spread, b + 1)
                nc.vector.reduce_max(top[x][:, :], layer2[x][:, SH * Q:SH * Q + P], AX.X).then_inc(top_ready, 1)

            def sum_denominators(b):
                dve.wait_ge(own_sums_ready, b + 1)
                dve.wait_ge(denom_safe_ready, b)
                nc.vector.reduce_sum(denom[:, :], own_sums[:, :].rearrange("p (r s) -> p r s", r=2),
                                     AX.X).then_inc(denom_ready, 2)

            def guard(b):
                dve.wait_ge(denom_ready, (b + 1) * 2)
                after(dve, inverse_ready, b)
                nc.vector.scalar_tensor_tensor(denom_safe[:, :], denom[:, :], 0.0, denom[:, :],
                                               ALU.is_equal, ALU.add).then_inc(denom_safe_ready, 1)

            def invert(b, x):
                dve.wait_ge(denom_safe_ready, b + 1)
                after(dve, pooled_ready, b - 1)
                nc.vector.reciprocal(inverse[x][:, :], denom_safe[:, :]).then_inc(inverse_ready, 1)

            def step(n, r, turn):
                x = r % 2
                steady = not isinstance(n, int)
                scores_here = steady or 2 <= n
                if scores_here:
                    scores_from_layer(n - 2, x)
                if steady or 4 <= n:
                    invert(n - 4, x)
                if not steady and n == 0:
                    dve.wait_ge(zeros_loaded, 16)
                dve.wait_ge(loaded[r][0], turn * 16 + (32 if r == 0 else 16))
                after(dve, layer1_done, n - 1)
                transpose_tokens(r, 0, 2)
                if not steady and n == 0:
                    place_weights()
                if scores_here:
                    max_of_partition(n - 2, x)
                dve.wait_ge(loaded[r][1], turn * 16 + 16)
                transpose_tokens(r, 2, 3)
                if scores_here:
                    max_of_batch(n - 2, x)
                transpose_tokens(r, 3, 4)
                if steady or 3 <= n:
                    guard(n - 3)

            steps(dve, step, NB)
            x = NB % 2
            scores_from_layer(NB - 2, x)
            invert(NB - 4, x)
            max_of_partition(NB - 2, x)
            max_of_batch(NB - 2, x)
            scores_from_layer(NB - 1, 1 - x)
            max_of_partition(NB - 1, 1 - x)
            guard(NB - 3)
            invert(NB - 3, 1 - x)
            max_of_batch(NB - 1, 1 - x)
            sum_denominators(NB - 2)
            guard(NB - 2)
            invert(NB - 2, x)
            sum_denominators(NB - 1)
            guard(NB - 1)
            invert(NB - 1, 1 - x)

        @block.tensor
        def _(pe):
            def spread_lengths(part, bank):
                at = left_parts[part][0][0]
                for col, n, first in left_parts[part]:
                    for i in range(I):
                        last = nc.tensor.matmul(bank[:, col - at:col - at + n],
                                                few_const[0:1, R_HOLDS + i * P:R_HOLDS + (i + 1) * P],
                                                lengths_f[0:1, first + i:first + i + I * (n - 1) + 1:I],
                                                start=(i == 0), stop=(i == I - 1))
                last.then_inc(lengths_spread, 1)

            def first_layer(n, x):
                after(pe, hidden_ready, n - 1)
                for j in range(J):
                    half = tokens_t[x][:, j // 2 * 2 * NJ * D:(j // 2 + 1) * 2 * NJ * D].rearrange(
                        "p (c g t b r) -> p g b c t r", g=2, t=T, b=HB, r=Q)
                    if j % 2 == 0:
                        pe.wait_ge(transposed, n * 3 + (1 if j == 0 else 3))
                    for b in range(HB):
                        last = nc.tensor.matmul(layer1[x][Q * j:Q * j + NQ * A, 0:NJ * Q], stationary1[:, b, :],
                                                half[:, j % 2, b], start=(b == 0), stop=(b == HB - 1),
                                                tile_position=(0, Q * j))
                last.then_inc(layer1_done, 1)

            def denominators(b, x):
                pe.wait_ge(weights_ready, b + 1)
                after(pe, all_sums_ready, b - 1)
                plain = weights_plain[x][:, :].rearrange("p (c s) -> p c s", c=PAIRS)
                for c in range(NQ):
                    single = NQ + c // 2
                    last = nc.tensor.matmul(denoms[x][Q * c:Q * c + 2 * ROWS, 0:4 * T * K], ind_rows,
                                            plain[:, c:single + 1:single - c, :],
                                            start=True, stop=True, tile_position=(0, Q * c))
                last.then_inc(denoms_done, 1)

            def sums_of_pairs(b, r, x, slots):
                if 0 in slots:
                    after(pe, pooled_ready, b - 1)
                buf = tokens[r][:, :].rearrange("p (c g t d) -> p c g t d", c=PAIRS, g=2, t=T)
                w = weights[x][:, :].rearrange("p (c t m) -> p c t m", c=PAIRS, t=T)
                for t in slots:
                    for c in range(NQ):
                        nc.tensor.matmul(sums[x][Q * c:Q * c + 2 * ROWS, 0:2 * D], w[:, c, t, :], buf[:, c, :, t, :],
                                         start=(t == 0), stop=(t == T - 1), tile_position=(0, Q * c))

            def sums_of_singles(r, x):
                buf = tokens[r][:, :].rearrange("p (c g t d) -> p c g t d", c=PAIRS, g=2, t=T)
                w = weights[x][:, :].rearrange("p (c t m) -> p c t m", c=PAIRS, t=T)
                for t in range(T):
                    for c in range(NQ):
                        pair, g = NQ + c // 2, c % 2
                        last = nc.tensor.matmul(sums[x][Q * c:Q * c + ROWS, 2 * D:3 * D],
                                                w[:, pair, t, g * ROWS:(g + 1) * ROWS], buf[:, pair, g, t, :],
                                                start=(t == 0), stop=(t == T - 1), tile_position=(0, Q * c))
                last.then_inc(sums_done, 1)

            def spread_max(b, x):
                pe.wait_ge(row_max_ready, b + 1)
                nc.tensor.transpose(layer2[x][:, SH * Q:SH * Q + P], row_max[x][:, 0:1].to_broadcast([P, P]),
                                    const[:, C_EYE:C_EYE + P]).then_inc(max_spread, 1)

            def second_layer(n, x):
                pe.wait_ge(hidden_ready, n + 1)
                after(pe, top_ready, n - 1)
                for half, n_slots in ((0, SH), (1, NJ - SH)):
                    last = nc.tensor.matmul(layer2[x][:, 0:n_slots * Q], stationary2[:, half, :],
                                            hidden[x][:, half * SH * Q:(half * SH + n_slots) * Q],
                                            start=(half == 0), stop=(half == 1))
                last.then_inc(layer2_done, 1)

            def step(n, r, turn):
                x = r % 2
                steady = not isinstance(n, int)
                layers = steady or n < NB
                summed = steady or n >= 2
                if layers:
                    first_layer(n, x)
                if not steady and n == 0:
                    spread_lengths(1, sums[0])
                    spread_lengths(2, sums[1])
                    pe.wait_ge(left_ready, 1)
                if not steady and n == 2:
                    pe.wait_ge(left_ready, 3)
                if not steady and n == NB - 1:
                    denominators(n - 2, x)
                    sums_of_pairs(n - 2, (r - 2) % RING, x, range(1))
                    spread_max(n - 1, 1 - x)
                    sums_of_pairs(n - 2, (r - 2) % RING, x, range(1, 3))
                    second_layer(n, x)
                    sums_of_pairs(n - 2, (r - 2) % RING, x, range(3, T))
                    sums_of_singles((r - 2) % RING, x)
                else:
                    if not steady and n == NB:
                        spread_max(n - 1, 1 - x)
                    if summed:
                        denominators(n - 2, x)
                        sums_of_pairs(n - 2, (r - 2) % RING, x, range(T))
                    if steady or 1 <= n < NB:
                        spread_max(n - 1, 1 - x)
                    if summed:
                        sums_of_singles((r - 2) % RING, x)
                    if layers:
                        second_layer(n, x)

            pe.wait_ge(cleared, CLEARS)
            pe.wait_ge(small_loaded, SMALL)
            for b in range(HB):
                for q in range(NQ):
                    nc.tensor.matmul(layer1[1][Q * q:Q * q + Q, b * A:(b + 1) * A], w1_rows[:, b * Q:(b + 1) * Q],
                                     const[0:A, C_EYE:C_EYE + A], start=True, stop=True, tile_position=(0, Q * q))
            nc.tensor.matmul(layer1[1][:, HB * A:HB * A + K + 1], few_const[:, R_HIDDEN:R_HIDDEN + P],
                             w2_b1_turned[:, :], start=True, stop=True).then_inc(weights_spread, 1)
            pe.wait_ge(lengths_ready, 1)
            spread_lengths(0, layer2[0])
            pe.wait_ge(stationary_ready, 3)
            steps(pe, step, NB + 2, peeled_end=RING)

        @block.scalar
        def _(act):
            act.dma_start(lengths[:, :], seq_len.unsqueeze(0)).then_inc(lengths_loaded, 16)
            act.dma_start(tokens[0][PU:P, :], zeros).then_inc(zeros_loaded, 16)
            act.dma_start(w1_rows[:, :], w1).then_inc(small_loaded, 16)
            with nc.allow_non_contiguous_dma(reason="a few weights"):
                act.dma_start(w2_b1_turned[:, 0:K], w2.rearrange("k a -> a k")).then_inc(small_loaded, 16)
                act.dma_start(w2_b1_turned[:, K:], b1.unsqueeze(1)).then_inc(small_loaded, 16)
            act.dma_start(b2_all[:, :], b2.unsqueeze(0).to_broadcast([P, K])).then_inc(b2_loaded, 16)

            def keep_left(part, bank):
                at = left_parts[part][0][0]
                end = left_parts[part][-1][0] + left_parts[part][-1][1]
                act.wait_ge(lengths_spread, part + 1)
                nc.scalar.activation(left[:, at:end], bank[:, 0:end - at],
                                     ACT.Identity, bias=const[:, C_START:C_START + 1]).then_inc(left_ready, 1)

            act.wait_ge(small_loaded, SMALL)
            keep_left(0, layer2[0])
            act.wait_ge(stationary_ready, 3)

            def add_up(n):
                act.wait_ge(own_sums_ready, n - 2)
                after(act, denom_safe_ready, n - 3)
                for part in range(2):
                    cols = slice(part * 2 * T * K, (part + 1) * 2 * T * K)
                    nc.scalar.activation(added[:, cols], own_sums[:, cols], ACT.Copy,
                                         accum_out=denom[:, part:part + 1]).then_inc(denom_ready, 1)

            def step(n, r, turn):
                x, y = r % 2, (r + 1) % 2
                if not isinstance(n, int) or 1 <= n < NB + 1:
                    act.wait_ge(layer1_done, n)
                    after(act, layer2_done, n - 2)
                    nc.scalar.activation(hidden[y][:, :], layer1[y][:, 0:NJ * Q], ACT.Tanh,
                                         bias=b1_rows[:, 0:1]).then_inc(hidden_ready, 1)
                if isinstance(n, int) and n == 1:
                    keep_left(1, sums[0])
                    keep_left(2, sums[1])
                late = isinstance(n, int) and n >= NB
                if not isinstance(n, int) or 3 <= n:
                    act.wait_ge(denoms_done, n - 2)
                    after(act, own_sums_ready, n - 3)
                    nc.scalar.copy(all_sums[:, :], denoms[y][:, 0:4 * T * K]).then_inc(all_sums_ready, 1)
                    if not late:
                        add_up(n)
                if not isinstance(n, int) or 2 <= n < NB + 2:
                    act.wait_ge(exp_bias_ready, n - 1)
                    after(act, sums_done, n - 3)
                    source = masked[x][:, 0:SLOTS * K].rearrange("p (s k) -> p s k", k=K)
                    for i in range(I):
                        nc.scalar.activation(
                            weights[x][:, :].rearrange("p (s i k) -> p s i k", i=I, k=K)[:, :, i, :],
                            source, ACT.Exp, bias=exp_bias[x][:, i:i + 1])
                    nc.scalar.activation(weights_plain[x][:, :], masked[x][:, 0:SLOTS * K], ACT.Exp,
                                         bias=exp_bias[x][:, I:I + 1]).then_inc(weights_ready, 1)
                if isinstance(n, int) and n == NB:
                    add_up(n)
                if not isinstance(n, int) or 3 <= n:
                    act.wait_ge(sums_done, n - 2)
                    act.wait_ge(inverse_ready, n - 2)
                    half, slot = (r - LAG) % RING // HALF, (r - LAG) % HALF
                    after(act, stored[half], (turn - (1 if r < LAG else 0)) * STORES)
                    for part, cols in enumerate((slice(0, 2 * D), slice(2 * D, 3 * D))):
                        ins = nc.scalar.activation(pooled[half][:, slot, cols], sums[y][:, cols], ACT.Copy,
                                                   scale=inverse[y][:, part:part + 1])
                    ins.then_inc(pooled_ready, 1)

            steps(act, step, NB + LAG)


_INS = ["r_behavior_embs", "r_pratical_seq_len", "L0_rec_W1_w", "L0_rec_W1_b", "L0_rec_W2_w", "L0_rec_W2_b"]


def kernel(**inputs):
    import numpy as _np
    import concourse.bacc as _bacc
    from concourse import mybir as _mybir
    from concourse.bass_utils import run_bass_kernel_spmd as _run

    nc = _bacc.Bacc("TRN2", target_bir_lowering=False, num_devices=1)
    arrays = {f"in_{name}_dram": _np.ascontiguousarray(inputs[name]) for name in _INS}
    arrays["in_consts_dram"], arrays["in_few_consts_dram"] = shape_constants(_np)
    arrays["in_zeros_dram"] = _np.zeros((P - PU, SLOTS * D), _np.float32)
    args = [nc.dram_tensor(name, a.shape, _mybir.dt.from_np(a.dtype), kind="ExternalInput").ap()
            for name, a in arrays.items()]
    args.append(nc.dram_tensor("out_0_dram", (N, K, D), F32, kind="ExternalOutput").ap())
    attention_pooling(nc, *args)
    r = _run(nc, [arrays], core_ids=[0])
    return r.results[0]["out_0_dram"]
```
